# Optimizing a Trainium2 kernel written in Bass

```python
import numpy as np
import jax
import jax.numpy as jnp

def _softmax(x, axis=-1):
    return jax.nn.softmax(x, axis=axis)

def _gelu(x):
    return jax.nn.gelu(x, approximate=True)

def _silu(x):
    return jax.nn.silu(x)

def _sigmoid(x):
    return jax.nn.sigmoid(x)

def _layernorm(x, axis=-1, eps=1e-05):
    m = jnp.mean(x, axis=axis, keepdims=True)
    v = jnp.var(x, axis=axis, keepdims=True)
    return (x - m) / jnp.sqrt(v + eps)

def _scatter_add(tgt, idx, src, axis=0):
    return tgt.at[idx].add(src)

def _segment_sum(src, seg, n):
    return jax.ops.segment_sum(src, seg, n)
kernel_name = 'mk_adaln_ffn_d1_seqx_r4_c6c283'

def setup_inputs(seed: int=0):
    np.random.seed(seed)
    _w = jnp.asarray

    def _rec_inputs():
        import jax
        import jax.numpy as jnp
        _rk = jax.random.key(seed)
        x = -0.0002928 + 1 * jax.random.normal(jax.random.fold_in(_rk, 1), (8, 256, 256), jnp.float32)
        _lenS = 256 - jax.random.randint(jax.random.fold_in(_rk, 7), (8,), 0, max(1, 256 // 4) + 1, jnp.int32)
        _lenS2 = 256 - jax.random.randint(jax.random.fold_in(_rk, 8), (8,), 0, max(1, 256 // 4) + 1, jnp.int32)
        cond_1024 = 0.000887014 + 1.03683 * jax.random.normal(jax.random.fold_in(_rk, 11), (8, 256), jnp.float32)
        return (x, cond_1024)
    x, cond_1024 = _rec_inputs()

    def _L0_cond_setup():
        import jax, jax.numpy as jnp
        import numpy as np
        TOP_K = 2
        N_EXPERTS = 8
        N_SHARED = 1
        EPS = 1e-09
        key = jax.random.key(seed)
        ks = jax.random.split(key, 10)
        B, T, d = (2, 512, 256)
        h_s, h_r, E = (512, 128, N_EXPERTS)
        return {'x': jax.random.normal(ks[0], (B, T, d), jnp.float32), 't_emb': jax.random.normal(ks[1], (B, d), jnp.float32), 'router_w': jax.random.normal(ks[2], (E, d), jnp.float32) * 0.01, 'router_t_w': jax.random.normal(ks[3], (E, d), jnp.float32) * 0.01, 'router_bias': jnp.zeros((E,), jnp.float32), 'sw1': jax.random.normal(ks[4], (h_s, d), jnp.float32) * 0.02, 'sw3': jax.random.normal(ks[5], (h_s, d), jnp.float32) * 0.02, 'sw2': jax.random.normal(ks[6], (d, h_s), jnp.float32) * 0.02, 'rw1': jax.random.normal(ks[7], (E, h_r, d), jnp.float32) * 0.02, 'rw2': jax.random.normal(ks[8], (E, d, h_r), jnp.float32) * 0.02}
    _L0_cond_all = _L0_cond_setup()
    _L0_cond_in = {k: v for k, v in _L0_cond_all.items() if k in ('router_w', 'router_t_w', 'router_bias', 'sw1', 'sw3', 'sw2', 'rw1', 'rw2')}
    del _L0_cond_all

    def _L0_ffn_setup():
        import jax, jax.numpy as jnp
        import numpy as np
        B, T, D, F, E = (2, 256, 256, 1024, 8)
        EPS = 1e-06
        key = jax.random.key(seed)
        k = jax.random.split(key, 5)
        scale = 0.02
        return {'x': jax.random.normal(k[0], (B, T, D), dtype=jnp.float32), 'rms_w': jnp.ones((D,), dtype=jnp.float32), 'gate_w': jax.random.normal(k[1], (E, D), dtype=jnp.float32) * scale, 'W1': jax.random.normal(k[2], (E, D, F), dtype=jnp.float32) * scale, 'b1': jnp.zeros((E, F), dtype=jnp.float32), 'W2': jax.random.normal(k[3], (E, F, D), dtype=jnp.float32) * scale, 'b2': jnp.zeros((E, D), dtype=jnp.float32)}
    _L0_ffn_all = _L0_ffn_setup()
    _L0_ffn_in = {k: v for k, v in _L0_ffn_all.items() if k in ('rms_w', 'gate_w', 'W1', 'b1', 'W2', 'b2')}
    del _L0_ffn_all
    return {'x': x, 'cond_1024': cond_1024, 'L0_cond_router_w': _L0_cond_in['router_w'], 'L0_cond_router_t_w': _L0_cond_in['router_t_w'], 'L0_cond_router_bias': _L0_cond_in['router_bias'], 'L0_cond_sw1': _L0_cond_in['sw1'], 'L0_cond_sw3': _L0_cond_in['sw3'], 'L0_cond_sw2': _L0_cond_in['sw2'], 'L0_cond_rw1': _L0_cond_in['rw1'], 'L0_cond_rw2': _L0_cond_in['rw2'], 'L0_ffn_rms_w': _L0_ffn_in['rms_w'], 'L0_ffn_gate_w': _L0_ffn_in['gate_w'], 'L0_ffn_W1': _L0_ffn_in['W1'], 'L0_ffn_b1': _L0_ffn_in['b1'], 'L0_ffn_W2': _L0_ffn_in['W2'], 'L0_ffn_b2': _L0_ffn_in['b2']}

def reference(x, cond_1024, L0_cond_router_w, L0_cond_router_t_w, L0_cond_router_bias, L0_cond_sw1, L0_cond_sw3, L0_cond_sw2, L0_cond_rw1, L0_cond_rw2, L0_ffn_rms_w, L0_ffn_gate_w, L0_ffn_W1, L0_ffn_b1, L0_ffn_W2, L0_ffn_b2):
    import jax
    import jax.numpy as jnp

    def _L0_cond_ref(x, t_emb, router_w, router_t_w, router_bias, sw1, sw3, sw2, rw1, rw2):
        import jax, jax.numpy as jnp
        import numpy as np
        TOP_K = 2
        N_EXPERTS = 8
        N_SHARED = 1
        EPS = 1e-09
        B, T, C = x.shape
        N = B * T
        x_flat = x.reshape(N, C)
        shared_out = jnp.einsum('nh,dh->nd', jax.nn.silu(x_flat @ sw1.T) * (x_flat @ sw3.T), sw2)
        t_bias = t_emb @ router_t_w.T
        t_bias_flat = jnp.broadcast_to(t_bias[:, None, :], (B, T, N_EXPERTS)).reshape(N, N_EXPERTS)
        s = jax.nn.sigmoid((x_flat @ router_w.T + t_bias_flat).astype(jnp.float32))
        sel_scores = s + router_bias
        _, topk_idx = jax.lax.top_k(sel_scores, TOP_K)
        s_sel = jnp.take_along_axis(s, topk_idx, axis=1)
        denom = jnp.sum(s_sel, axis=1, keepdims=True)
        gates = jnp.where(denom > EPS, s_sel / (denom + EPS), 1.0 / TOP_K).astype(x.dtype)
        combine = jnp.sum(gates[:, :, None] * jax.nn.one_hot(topk_idx, N_EXPERTS, dtype=x.dtype), axis=1)
        H = jax.nn.gelu(jnp.einsum('nd,ehd->enh', x_flat, rw1), approximate=False)
        O = jnp.einsum('enh,edh->end', H, rw2)
        routed_out = jnp.einsum('end,ne->nd', O, combine)
        out = (shared_out + routed_out) / (N_SHARED + TOP_K)
        return out.reshape(B, T, C)

    def _L0_ffn_ref(x, rms_w, gate_w, W1, b1, W2, b2):
        import jax, jax.numpy as jnp
        import numpy as np
        B, T, D, F, E = (2, 256, 256, 1024, 8)
        EPS = 1e-06
        ms = jnp.mean(x * x, axis=-1, keepdims=True)
        xn = x * jax.lax.rsqrt(ms + EPS) * rms_w
        logits = jnp.einsum('btd,ed->bte', xn, gate_w)
        scores = jax.nn.softmax(logits, axis=-1)
        top1_idx = jnp.argmax(scores, axis=-1)
        top1_score = jnp.max(scores, axis=-1)
        out = jnp.zeros_like(xn)
        for e in range(E):
            h = jax.nn.silu(jnp.einsum('btd,df->btf', xn, W1[e]) + b1[e])
            ye = jnp.einsum('btf,fd->btd', h, W2[e]) + b2[e]
            out = jnp.where((top1_idx == e)[..., None], ye, out)
        return out * top1_score[..., None]
    x = x + _L0_ffn_ref(_L0_cond_ref(x, cond_1024, L0_cond_router_w, L0_cond_router_t_w, L0_cond_router_bias, L0_cond_sw1, L0_cond_sw3, L0_cond_sw2, L0_cond_rw1, L0_cond_rw2), L0_ffn_rms_w, L0_ffn_gate_w, L0_ffn_W1, L0_ffn_b1, L0_ffn_W2, L0_ffn_b2)
    return x

_drawn_inputs = setup_inputs


def setup_inputs(seed=0):
    import zlib

    import numpy as np

    out = dict(_drawn_inputs(seed))
    spreads = {'L0_cond_router_bias': (0.0, 0.1),
     'L0_ffn_rms_w': (1.0, 0.6),
     'L0_ffn_b1': (0.0, 0.8),
     'L0_ffn_b2': (0.0, 0.396)}
    factors = {'cond_1024': 3.836, 'L0_cond_router_w': 3.396, 'L0_cond_router_t_w': 3.195}
    for name, (base, spread) in spreads.items():
        noise = np.random.default_rng([zlib.crc32(name.encode()), seed]).standard_normal(out[name].shape)
        drawn = base * np.exp(spread * noise) if base else spread * noise
        out[name] = jnp.asarray(drawn.astype(out[name].dtype))
    for name, factor in factors.items():
        out[name] = (out[name] * factor).astype(out[name].dtype)
    return out
```

```python
import numpy as np
from contextlib import ExitStack

import concourse.bass as bass
from concourse import mybir

F32 = mybir.dt.float32
F32R = mybir.dt.float32r
BF16 = mybir.dt.bfloat16
I32 = mybir.dt.int32
ALU = mybir.AluOpType
ACT = mybir.ActivationFunctionType
AX = mybir.AxisListType.X


def build(nc, x, xT, condT, routerT, router_tT, router_bias, sw1T, sw3T, sw2T, rw1T, rw2T,
          rms_row, gateT, W1, b1, W2, b2, out, scratch):
    P = 128
    N, D = x.shape
    E = router_bias.shape[0]
    KD = D // P
    T = N // P
    BT = 4
    NB = T // BT
    BC = BT * P
    HS = sw1T.shape[2]
    CS = HS // P
    STEPS = CS + E
    F = W1.shape[2]
    CF = F // P
    BPE = T // (N // condT.shape[2] // P) // NB
    TPB = BT // BPE
    NBATCH = condT.shape[2]
    ST = T + E - 1
    JC = ST + 1
    EPS1, EPS2 = 1e-9, 1e-6
    NRC = 23
    PC = 1024
    NP1 = 7
    NPE = 4
    SLOT = 2 * NPE * PC
    NSLOT = 3
    S1W = (NSLOT - 1) * SLOT
    S1L = S1W + NP1 * PC
    BW = F + D
    NCOL = 6
    C_NEED, C_WOFF, C_BOFF, C_PREP, C_POFF, C_PEXP = range(NCOL)
    MOST = (E, (NSLOT - 1) * SLOT, (NSLOT - 1) * BW, 1, (NSLOT - 1) * SLOT, E - 1)
    RX = 4

    ctx = ExitStack()
    with ctx:
        def sb(name, cols, dt=F32):
            return ctx.enter_context(nc.sbuf_tensor(name, [P, cols], dt))

        def ps(name):
            return ctx.enter_context(nc.psum_tensor(name, [P, 512], F32))

        def sem(name):
            return ctx.enter_context(nc.semaphore(name))

        WA = sb("WA", S1L + NP1 * PC, F32R)
        STG = sb("STG", 2 * PC)
        BIAS = sb("BIAS", NSLOT * BW)
        XR = sb("XR", KD * BC)
        XH = sb("XH", KD * BC, F32R)
        XL = sb("XL", KD * BC, F32R)
        HF = sb("HF", 2 * F)
        HH = sb("HH", 2 * F, F32R)
        HL = sb("HL", 2 * F, F32R)
        AU = sb("AU", 2 * F)
        XG = sb("XG", RX * 2 * D)
        OX = sb("OX", 6 * D)
        OUTB, YB = OX[:, 0:RX * D], OX[:, RX * D:(RX + 1) * D]
        ACC, U = AU[:, 0:BT * D], AU[:, BT * D:2 * BT * D]
        UT = XG[:, 0:KD * BC]
        RMSB = sb("RMSB", D)
        RW = sb("RW", KD * E)
        RTW = sb("RTW", KD * E)
        GW = sb("GW", KD * E)
        CT = sb("CT", KD * NBATCH)
        TB = sb("TB", NBATCH * E)
        RB = sb("RB", E)
        ONES = sb("ONES", P)
        ONEB = sb("ONEB", P, BF16)
        TRI = sb("TRI", P, BF16)
        IDENT = sb("IDENT", P)
        IOTA = sb("IOTA", P)
        REV = sb("REV", E)
        THR = sb("THR", JC + 1)
        TOK = sb("TOK", T)
        LG = sb("LG", BT * E)
        SG = sb("SG", BT * E)
        SEL = sb("SEL", BT * E)
        K1 = sb("K1", BT * E)
        K2 = sb("K2", BT * E)
        OH1 = sb("OH1", BT * E)
        OH2 = sb("OH2", BT * E)
        R1 = sb("R1", 8 * BT)
        CMB = sb("CMB", T * E)
        MS = sb("MS", T)
        OHB = sb("OHB", T * E, BF16)
        AOH = HF
        VV = OX[:, 0:T * 4 * ST]
        W8 = [XR[:, n * T * E:(n + 1) * T * E] for n in range(4)]
        TE = XR[:, 4 * T * E:5 * T * E]
        TJ = XR[:, 5 * T * E:5 * T * E + JC * E]
        CE = XR[:, 5 * T * E + JC * E:5 * T * E + JC * E + 5 * E]
        TF = XR[:, 7 * T * E:7 * T * E + 4 * JC]
        GE = XG[:, KD * BC:KD * BC + T * (JC + 1)]
        RV = XG[:, 3 * BC:3 * BC + 8 * T]
        LOG = XG[:, 3 * BC + T * E:3 * BC + 2 * T * E]
        MS2 = XG[:, 3 * BC + 2 * T * E:3 * BC + 2 * T * E + 2 * T]
        SIDF = XG[:, 3 * BC + 2 * T * E + 2 * T:3 * BC + 2 * T * E + 2 * T + ST]
        MSQ, SQ = MS2[:, 0:T], MS2[:, T:2 * T]
        PCB = HF[:, 0:KD * NBATCH * E]
        TAB = sb("TAB", JC * NCOL, I32)
        SRT = sb("SRT", 4 * ST)
        GID = sb("GID", ST, I32)
        SID = sb("SID", ST, I32)
        GI = sb("GI", RX, I32)
        SI = sb("SI", RX, I32)

        PF = [ps(f"PF{i}") for i in range(4)]
        PS = [ps(f"PS{i}") for i in range(4)]

        s_const = sem("const_loaded")
        s_x = sem("x_block_loaded")
        s_stg = [sem(f"staging{i}_loaded") for i in range(2)]
        s_bias = sem("bias_loaded")
        s_hi = sem("expert_hi_loaded")
        s_xcopy = sem("x_copied_to_scratch")
        s_ust = sem("u_stored")
        s_gather = [sem(f"tile_gathered{i}") for i in range(RX)]
        s_scatter = [sem(f"rows_stored{i}") for i in range(RX)]
        s_pool = sem("pool_constants")
        s_set = sem("dve_setup")
        s_tb = sem("t_bias_product")
        s_wsplit = sem("s1_weights_split")
        s_xsplit = sem("x_split")
        s_r = sem("router1_product")
        s_rl = sem("router1_logits")
        s_rs = sem("router1_sigmoid")
        s_rc = sem("router1_chain")
        s_f = sem("f_product")
        s_act = sem("activated")
        s_hact = sem("act_hi")
        s_mul = sem("shared_gated")
        s_hdve = sem("dve_hi")
        s_h = sem("h_split")
        s_s = sem("s_bank_done")
        s_comb = sem("combined")
        s_u = sem("u_done")
        s_ms = sem("mean_square")
        s_t = sem("u_transposed")
        s_ut = sem("uT_copied")
        s_l = sem("router2_product")
        s_lc = sem("router2_logits_copied")
        s_v = sem("route_chain")
        s_va = sem("route_act")
        s_rank = sem("rank_product")
        s_sort = sem("sort_product")
        s_aoh = sem("place_onehot")
        s_msq = sem("mean_squares_ready")
        s_diff = sem("logits_less_max")
        s_ohb = sem("best_expert_onehot")
        s_route = sem("routing_done")
        s_lo = sem("expert_piece_low")
        s_gi = sem("gather_index")
        s_held = sem("pool_wait_carrier")
        s_si = sem("scatter_index")
        s_xt = sem("xg_transposed")
        s_xh = sem("xg_hi")
        s_xl = sem("xg_split")
        s_f2 = sem("f2_half")
        s_z = sem("z_half")
        s_ht = sem("h_transposed_half")
        s_si2 = sem("silu_half")
        s_h2h = sem("h2_hi_half")
        s_h2 = sem("h2_split_half")
        s_y = sem("y_product")
        s_yb = sem("y_biased")
        s_o = sem("out_rows")

        SLOTS = [("R", 0)]
        for i in range(CS):
            SLOTS += [("a", i), ("b", i)]
        SLOTS += [("T", 0), ("T", 1), ("e", 0), ("e", 1), ("L", 0)] + [("e", i) for i in range(2, E)]
        NSL = len(SLOTS)
        assert NSL % 4 == 0

        def slot_of(kind, i):
            return SLOTS.index((kind, i))

        def f_bank(kind, i):
            return PF[slot_of(kind, i) % 4]

        def f_event(b, kind, i):
            idx = 2 * i + (kind == "b") if kind in "ab" else 2 * CS + i
            return (2 * CS + E) * b + idx + 1

        def wait_slot_read(eng, b, kind, i, first):
            s = slot_of(kind, i) - 4
            while True:
                back = s < 0
                if back and first:
                    return
                k, n = SLOTS[s % NSL]
                if first and k in "TL":
                    s -= 4
                    continue
                bb = b - 1 if back else b
                if k == "R":
                    eng.wait_ge(s_rl, bb + 1)
                elif k == "a":
                    eng.wait_ge(s_act, STEPS * bb + n + 1)
                elif k == "e":
                    eng.wait_ge(s_act, STEPS * bb + CS + n + 1)
                elif k == "b":
                    eng.wait_ge(s_mul, CS * bb + n + 1)
                elif k == "T":
                    eng.wait_ge(s_ut, KD * (bb - 1) + n + 1)
                else:
                    eng.wait_ge(s_lc, bb)
                return

        COMBS = BT // 2 + BT * E

        def comb_event(b, i, t):
            return COMBS * b + (t // 2 + 1 if i == CS - 1 else BT // 2 + BT * (i - CS) + t + 1)

        SBANKS = CS - 1 + 2 * (1 + E)

        def s_event(b, i, half):
            if i < 0:
                return s_event(b - 1, i + STEPS, half)
            return SBANKS * b + (i + 1 if i < CS - 1 else CS - 1 + 2 * (i - CS + 1) + half + 1)

        def s_pair(i):
            return PS[0:2] if i < CS or (i - CS) % 2 else PS[2:4]

        def hi1(piece, a, n):
            return WA[:, S1W + piece * PC + a:S1W + piece * PC + a + n]

        def lo1(piece, a, n):
            return WA[:, S1L + piece * PC + a:S1L + piece * PC + a + n]

        def w_first(kind, i, k):
            if kind == "a":
                return 0, k * HS + i * P
            if kind == "b":
                return 1, k * HS + i * P
            return 3 + k, i * P

        def w_second(i):
            return (2, i * D) if i < CS else (5 + (i - CS) // 4, (i - CS) % 4 * D)

        x_tok = x.rearrange("(n p) d -> p n d", p=P)
        scr_u = scratch.rearrange("(b t p) c -> p b t c", t=BT, p=P)
        w1_v = W1.rearrange("e (k p) f -> p e k f", p=P)
        w2_v = W2.rearrange("e (c p) d -> p e c d", p=P)

        HEAD, TURNS = 3, (ST - 6) // 4

        def sorted_tiles(eng, step):
            for c in range(HEAD):
                step(0, c)
            with eng.Fori(0, TURNS) as i:
                for c in range(HEAD, HEAD + 4):
                    step(i, c)
            for c in range(HEAD + 4 * TURNS, ST):
                step(0, c)

        block = ctx.enter_context(nc.Block())

        @block.sync
        def _(sp):
            sp.dma_start(RW[:, :], routerT.rearrange("p k e -> p (k e)")).then_inc(s_const, 16)
            sp.dma_start(RTW[:, :], router_tT.rearrange("p k e -> p (k e)")).then_inc(s_const, 16)
            sp.dma_start(CT[:, :], condT.rearrange("p k b -> p (k b)")).then_inc(s_const, 16)
            sp.dma_start(RB[:, :], router_bias.rearrange("(a e) -> a e", a=1).broadcast_to([P, E])).then_inc(s_const, 16)
            sp.dma_start(GW[:, :], gateT.rearrange("p k e -> p (k e)")).then_inc(s_const, 16)
            sp.dma_start(RMSB[:, :], rms_row.rearrange("(a d) -> a d", a=1).broadcast_to([P, D])).then_inc(s_const, 16)

            def load_x(b):
                if b:
                    sp.wait_ge(s_r, b)
                    sp.wait_ge(s_xsplit, 2 * b)
                sp.dma_start(XR[:, :].rearrange("p (k c) -> p k c", k=KD),
                             xT[:, :, b * BC:(b + 1) * BC]).then_inc(s_x, 16)

            def stage(n, src):
                if n >= 2:
                    if n - 2 < NP1:
                        sp.wait_ge(s_wsplit, 2 * (n - 2) + 2)
                    else:
                        sp.wait_ge(s_lo, n - 2 - NP1 + 1)
                dst = STG[:, n % 2 * PC:(n % 2 + 1) * PC]
                if len(src.shape) == 3:
                    dst = dst.rearrange("p (k c) -> p k c", k=src.shape[1])
                sp.dma_start(dst, src).then_inc(s_stg[n % 2], 16)

            load_x(0)
            stage(0, sw1T)
            stage(1, sw3T)
            stage(2, sw2T)
            stage(3, rw1T[:, 0, :])
            stage(4, rw1T[:, 1, :])
            stage(5, rw2T[:, 0:E // 2, :])
            stage(6, rw2T[:, E // 2:E, :])
            load_x(1)
            sp.dma_start(scratch[:, D:2 * D], x).then_inc(s_xcopy, 16)

            def stage_expert(e):
                n = NP1 + NPE * e
                for k in range(KD):
                    stage(n + k, w1_v[:, e, k, :])
                for h in range(2):
                    stage(n + 2 + h, w2_v[:, e, h * CF // 2:(h + 1) * CF // 2, :])

            def load_bias(e):
                if e >= NSLOT:
                    sp.wait_ge(s_hi, 32 * (e + 1))
                if e:
                    sp.wait_ge(s_bias, 32 * e)
                o = e % NSLOT * BW
                sp.dma_start(BIAS[:, o:o + F], b1[e:e + 1, :].broadcast_to([P, F])).then_inc(s_bias, 16)
                sp.dma_start(BIAS[:, o + F:o + BW], b2[e:e + 1, :].broadcast_to([P, D])).then_inc(s_bias, 16)

            stage_expert(0)
            load_bias(0)
            load_x(2)
            stage_expert(1)
            load_bias(1)
            load_x(3)
            for e in range(2, E):
                stage_expert(e)
                load_bias(e)
            sp.wait_ge(s_ust, 16 * NB)
            sp.wait_ge(s_xcopy, 16)

        @block.gpsimd
        def _(pool):
            pool.memset(ONES[:, :], 1.0).then_inc(s_pool, 1)
            pool.memset(ONEB[:, :], 1.0).then_inc(s_pool, 1)
            pool.memset(TRI[:, :], 1.0).then_inc(s_pool, 1)
            pool.memset(IDENT[:, :], 0.0).then_inc(s_pool, 1)
            pool.iota(IOTA[:, :], [[1, P]], base=0, channel_multiplier=0,
                      allow_small_or_imprecise_dtypes=True).then_inc(s_pool, 1)
            pool.iota(REV[:, :], [[-1, E]], base=E, channel_multiplier=0,
                      allow_small_or_imprecise_dtypes=True).then_inc(s_pool, 1)
            pool.iota(THR[:, :], [[P, JC + 1]], base=0, channel_multiplier=0,
                      allow_small_or_imprecise_dtypes=True).then_inc(s_pool, 1)
            pool.iota(TOK[:, :], [[P, T]], base=0, channel_multiplier=1,
                      allow_small_or_imprecise_dtypes=True).then_inc(s_pool, 1)
            pool.wait_ge(s_pool, 8)
            pool.affine_select(out=TRI[:, :], in_=TRI[:, :], compare_op=ALU.is_gt, fill=0.0, base=0,
                               pattern=[[1, P]], channel_multiplier=-1).then_inc(s_pool, 1)
            pool.affine_select(out=IDENT[:, :], in_=IDENT[:, :], compare_op=ALU.not_equal, fill=1.0, base=0,
                               pattern=[[-1, P]], channel_multiplier=1).then_inc(s_pool, 1)

            def load_hi(e, base):
                hi = WA[:, bass.ds(base, NPE * PC)]
                pool.dma_start(hi[:, 0:2 * PC].rearrange("p (e k f) -> p e k f", e=1, k=KD),
                               w1_v[:, bass.ds(e, 1), :, :]).then_inc(s_hi, 16)
                pool.dma_start(hi[:, 2 * PC:4 * PC].rearrange("p (e c d) -> p e c d", e=1, c=CF),
                               w2_v[:, bass.ds(e, 1), :, :]).then_inc(s_hi, 16)

            def split(e, q, base):
                n = NP1 + q
                pool.wait_ge(s_stg[n % 2], 16 * (n // 2 + NPE // 2 * e + 1))
                if q == 0:
                    pool.wait_ge(s_hi, 32 * (e + 1))
                ins = pool.tensor_tensor(WA[:, bass.ds(base + (NPE + q) * PC, PC)],
                                         STG[:, n % 2 * PC:(n % 2 + 1) * PC],
                                         WA[:, bass.ds(base + q * PC, PC)].bitcast(F32), ALU.subtract)
                ins.then_inc(s_lo, 1)

            for e in range(2):
                load_hi(e, e * SLOT)
                for q in range(NPE):
                    split(e, q, e * SLOT)
            pool.wait_ge(s_s, SBANKS * NB)
            load_hi(2, 2 * SLOT)

            def gather(i, c):
                j, r = 4 * i + c, c % RX
                pool.tensor_copy(GI[:, r:r + 1], GID[:, bass.ds(j, 1)]).then_inc(s_gi, 1)
                pool.wait_ge(s_gi, j + 1)
                pool.sem_inc(s_held, 1)
                pool.indirect_dma_start(XG[:, r * 2 * D:(r + 1) * 2 * D], None, scratch,
                                        bass.IndirectOffsetOnAxis(ap=GI[:, r:r + 1], axis=0)
                                        ).then_inc(s_gather[r], 16)

            def scatter(i, c):
                j, r = 4 * i + c, c % RX
                pool.wait_ge(s_o, j + 1)
                pool.tensor_copy(SI[:, r:r + 1], SID[:, bass.ds(j, 1)]).then_inc(s_si, 1)
                pool.wait_ge(s_si, j + 1)
                pool.sem_inc(s_held, 1)
                pool.indirect_dma_start(out, bass.IndirectOffsetOnAxis(ap=SI[:, r:r + 1], axis=0),
                                        OUTB[:, r * D:(r + 1) * D], None,
                                        bounds_check=N - 1, oob_is_err=False).then_inc(s_scatter[r], 16)

            def tab(a, i, c):
                return pool.value_load(TAB[0:1, bass.ds((4 * i + c) * NCOL + a, 1)], min_val=0, max_val=MOST[a])

            def prepare(i, c, pieces):
                with pool.If(tab(C_PREP, i, c) > 0):
                    e, base = tab(C_PEXP, i, c), tab(C_POFF, i, c)
                    if pieces:
                        for q in pieces:
                            split(e, q, base)
                    else:
                        pool.wait_ge(s_o, 4 * i + c)
                        pool.sem_inc(s_held, 1)
                        load_hi(e, base)

            def step(i, c):
                if c >= 2:
                    scatter(i, c - 2)
                if c + 2 < ST:
                    gather(i, c + 2)
                if c >= 3:
                    prepare(i, c - 2, (2, 3))
                if c >= 2:
                    prepare(i, c - 1, (0, 1))
                if c >= 1:
                    prepare(i, c, ())

            for q in range(NPE):
                split(2, q, 2 * SLOT)
            pool.wait_ge(s_route, 1)
            pool.wait_ge(s_ust, 16 * NB)
            pool.wait_ge(s_xcopy, 16)
            gather(0, 0)
            gather(0, 1)
            sorted_tiles(pool, step)
            for c in (ST - 2, ST - 1):
                scatter(0, c)
            for r in range(RX):
                pool.wait_ge(s_scatter[r], 16 * len(range(r, ST, RX)))

        @block.scalar
        def _(act):
            def sigmoid(b, first):
                act.wait_ge(s_rl, b + 1)
                if not first:
                    act.wait_ge(s_rc, NRC * b)
                act.activation(SG[:, :], LG[:, :], ACT.Sigmoid).then_inc(s_rs, 1)

            def activate(b, i, func, bank, event, first):
                act.wait_ge(s_f, event)
                if i >= 4 or not first:
                    act.wait_ge(s_h, STEPS * b + i - 3)
                h = i % 4 * BC
                act.activation(HF[:, h:h + BC], bank[:, :], func).then_inc(s_act, 1)

            def high(b, i):
                act.wait_ge(s_act, STEPS * b + i + 1)
                act.wait_ge(s_s, s_event(b, i - 4, 1))
                h = i % 4 * BC
                act.activation(HH[:, h:h + BC], HF[:, h:h + BC], ACT.Copy).then_inc(s_hact, 1)

            def mean_squares(b):
                act.wait_ge(s_comb, COMBS * (b + 1))
                for t in range(BT):
                    act.activation(OX[:, t * D:(t + 1) * D], ACC[:, t * D:(t + 1) * D], ACT.Square,
                                   accum_out=MS[:, bass.ds(BT * b + t, 1)]).then_inc(s_ms, 1)
                act.wait_ge(s_ms, BT * (b + 1))

            def store_u(b):
                act.wait_ge(s_u, b + 1)
                act.dma_start(scr_u[:, bass.ds(b, 1), :, 0:D],
                              U.rearrange("p (b t d) -> p b t d", b=1, t=BT)).then_inc(s_ust, 16)

            def copy_ut(b):
                for k in range(KD):
                    act.wait_ge(s_t, KD * b + k + 1)
                    act.activation(UT[:, k * BC:(k + 1) * BC], f_bank("T", k)[:, :], ACT.Copy).then_inc(s_ut, 1)

            def body(b, first):
                sigmoid(b, first)
                for i in range(CS):
                    activate(b, i, ACT.Silu, f_bank("a", i), f_event(b, "a", i), first)
                    if i == 1 and not first:
                        mean_squares(b - 1)
                        store_u(b - 1)
                if not first:
                    copy_ut(b - 1)
                for e in range(E):
                    activate(b, CS + e, ACT.Gelu, f_bank("e", e), f_event(b, "e", e), first)
                    high(b, CS + e)

            body(0, True)
            with act.Fori(1, NB) as b:
                body(b, False)
            mean_squares(NB - 1)
            store_u(NB - 1)
            copy_ut(NB - 1)

            act.wait_ge(s_msq, 1)
            act.activation(SQ, MSQ, ACT.Sqrt).then_inc(s_va, 1)
            act.wait_ge(s_diff, 1)
            act.activation(W8[2], W8[1], ACT.Exp).then_inc(s_va, 1)

            def high_x(i, c):
                act.wait_ge(s_xt, 4 * i + c + 1)
                x0 = c % 2 * D
                act.activation(XH[:, x0:x0 + D], PF[2][:, 0:D], ACT.Copy).then_inc(s_xh, 1)

            def step(i, c):
                j = 4 * i + c
                if c + 1 < ST:
                    high_x(i, c + 1)
                h0 = c % 2 * F
                for h in range(2):
                    act.wait_ge(s_ht, 2 * j + h + 1)
                    if c >= 2:
                        act.wait_ge(s_h2, 2 * j + h - 3)
                    a = h0 + h * 512
                    act.activation(HF[:, a:a + 512], PS[2 + h][:, :], ACT.Silu).then_inc(s_si2, 1)
                if c >= 2:
                    act.wait_ge(s_y, j - 1)
                for h in range(2):
                    act.wait_ge(s_si2, 2 * j + h + 1)
                    a = h0 + h * 512
                    act.activation(HH[:, a:a + 512], HF[:, a:a + 512], ACT.Copy).then_inc(s_h2h, 1)

            high_x(0, 0)
            sorted_tiles(act, step)

        @block.vector
        def _(dve):
            dve.wait_ge(s_const, 16 * 6)
            for k in range(KD):
                dve.tensor_tensor(
                    PCB[:, k * NBATCH * E:(k + 1) * NBATCH * E].rearrange("p (b e) -> p b e", e=E),
                    CT[:, k * NBATCH:(k + 1) * NBATCH].unsqueeze(2).broadcast_to([P, NBATCH, E]),
                    RTW[:, k * E:(k + 1) * E].unsqueeze(1).broadcast_to([P, NBATCH, E]),
                    ALU.mult).then_inc(s_set, 1)

            def split_x(b, first):
                dve.wait_ge(s_x, 16 * (b + 1))
                if not first:
                    dve.wait_ge(s_f, (2 * CS + E) * b)
                dve.tensor_copy(XH[:, :], XR[:, :]).then_inc(s_xsplit, 1)
                dve.wait_ge(s_xsplit, 2 * b + 1)
                dve.tensor_tensor(XL[:, :], XR[:, :], XH[:, :].bitcast(F32), ALU.subtract).then_inc(s_xsplit, 1)

            def split_w(n):
                dve.wait_ge(s_stg[n % 2], 16 * (n // 2 + 1))
                src = STG[:, n % 2 * PC:(n % 2 + 1) * PC]
                dve.tensor_copy(hi1(n, 0, PC), src).then_inc(s_wsplit, 1)
                dve.wait_ge(s_wsplit, 2 * n + 1)
                dve.tensor_tensor(lo1(n, 0, PC), src, hi1(n, 0, PC).bitcast(F32), ALU.subtract).then_inc(s_wsplit, 1)

            def logits1(b):
                dve.wait_ge(s_r, b + 1)
                dve.tensor_tensor(LG[:, :].rearrange("p (m t e) -> p m t e", m=BPE, e=E),
                                  f_bank("R", 0)[:, 0:BT * E].rearrange("p (m t e) -> p m t e", m=BPE, e=E),
                                  TB[:, bass.ds(b * BPE * E, BPE * E)].rearrange("p (m e) -> p m e", e=E)
                                  .unsqueeze(2).broadcast_to([P, BPE, TPB, E]), ALU.add).then_inc(s_rl, 1)

            def route1(b):
                k = [0]

                def link(ins):
                    k[0] += 1
                    ins.then_inc(s_rc, 1)
                    dve.wait_ge(s_rc, NRC * b + k[0])

                def v3(a):
                    return a[:, 0:BT * E].rearrange("p (t e) -> p t e", e=E)

                def row(n):
                    return R1[:, n * BT:(n + 1) * BT]

                def wide(n):
                    return row(n).unsqueeze(2).broadcast_to([P, BT, E])

                bias = RB[:, :].unsqueeze(1).broadcast_to([P, BT, E])
                rev = REV[:, :].unsqueeze(1).broadcast_to([P, BT, E])
                dve.wait_ge(s_rs, b + 1)
                link(dve.tensor_tensor(v3(SEL), v3(SG), bias, ALU.add))
                for n, oh in enumerate((OH1, OH2)):
                    link(dve.tensor_reduce(row(0), v3(SEL), AX, ALU.max))
                    link(dve.tensor_tensor(v3(K1), v3(SEL), wide(0), ALU.is_equal))
                    link(dve.tensor_tensor(v3(K2), v3(K1), rev, ALU.mult))
                    link(dve.tensor_reduce(row(1), v3(K2), AX, ALU.max))
                    link(dve.tensor_tensor(v3(oh), v3(K2), wide(1), ALU.is_equal))
                    if n == 0:
                        link(dve.scalar_tensor_tensor(SEL[:, :], OH1[:, :], -1e30, SEL[:, :], ALU.mult, ALU.add))
                link(dve.tensor_tensor(OH1[:, :], OH1[:, :], OH2[:, :], ALU.add))
                link(dve.tensor_tensor(K1[:, :], SG[:, :], OH1[:, :], ALU.mult))
                link(dve.tensor_reduce(row(2), v3(K1), AX, ALU.add))
                link(dve.tensor_scalar(row(3), row(2), EPS1, None, ALU.add))
                link(dve.reciprocal(row(4), row(3)))
                link(dve.tensor_scalar(row(5), row(2), EPS1, None, ALU.is_gt))
                link(dve.scalar_tensor_tensor(row(6), row(4), 1.0 / 3.0, row(5), ALU.mult, ALU.mult))
                link(dve.tensor_scalar(row(7), row(5), -1.0 / 6.0, 1.0 / 6.0, ALU.mult, ALU.add))
                link(dve.tensor_tensor(v3(K1), v3(K1), wide(6), ALU.mult))
                link(dve.tensor_tensor(v3(K2), v3(OH1), wide(7), ALU.mult))
                link(dve.tensor_tensor(CMB[:, bass.ds(b * BT * E, BT * E)], K1[:, :], K2[:, :], ALU.add))
                assert k[0] == NRC

            def gated(b, i, first):
                h = i % 4 * BC
                dve.wait_ge(s_act, STEPS * b + i + 1)
                dve.wait_ge(s_f, f_event(b, "b", i))
                dve.tensor_tensor(HF[:, h:h + BC], HF[:, h:h + BC], f_bank("b", i)[:, :], ALU.mult).then_inc(s_mul, 1)
                dve.wait_ge(s_mul, CS * b + i + 1)
                if not first:
                    dve.wait_ge(s_s, s_event(b, i - 4, 1))
                dve.tensor_copy(HH[:, h:h + BC], HF[:, h:h + BC]).then_inc(s_hdve, 1)
                dve.wait_ge(s_hdve, CS * b + i + 1)
                dve.tensor_tensor(HL[:, h:h + BC], HF[:, h:h + BC], HH[:, h:h + BC].bitcast(F32),
                                  ALU.subtract).then_inc(s_h, 1)

            def low(b, i):
                h = i % 4 * BC
                dve.wait_ge(s_hact, E * b + i - CS + 1)
                dve.tensor_tensor(HL[:, h:h + BC], HF[:, h:h + BC], HH[:, h:h + BC].bitcast(F32),
                                  ALU.subtract).then_inc(s_h, 1)

            def combine(b, i, first):
                if i == CS - 1:
                    if not first:
                        dve.wait_ge(s_ms, BT * b)
                    for h in range(2):
                        dve.wait_ge(s_s, s_event(b, i, h))
                        dve.tensor_scalar(ACC[:, h * 512:(h + 1) * 512], s_pair(i)[h][:, :], 1.0 / 3.0, None,
                                          ALU.mult).then_inc(s_comb, 1)
                    return
                for t in range(BT):
                    if t % 2 == 0:
                        dve.wait_ge(s_s, s_event(b, i, t // 2))
                    dve.wait_ge(s_comb, comb_event(b, i - 1, t))
                    acc = ACC[:, t * D:(t + 1) * D]
                    dve.scalar_tensor_tensor(acc, s_pair(i)[t // 2][:, t % 2 * D:(t % 2 + 1) * D],
                                             CMB[:, bass.ds((BT * b + t) * E + i - CS, 1)], acc,
                                             ALU.mult, ALU.add).then_inc(s_comb, 1)

            def times_rms(b):
                dve.wait_ge(s_comb, COMBS * (b + 1))
                dve.tensor_tensor(U.rearrange("p (t d) -> p t d", d=D), ACC.rearrange("p (t d) -> p t d", d=D),
                                  RMSB[:, :].unsqueeze(1).broadcast_to([P, BT, D]), ALU.mult).then_inc(s_u, 1)

            def logits2(b):
                dve.wait_ge(s_l, b + 1)
                dve.tensor_copy(LOG[:, bass.ds(b * BT * E, BT * E)], f_bank("L", 0)[:, 0:BT * E]).then_inc(s_lc, 1)

            def body(b, first):
                split_x(b, first)
                if first:
                    split_w(0)
                    split_w(1)
                    dve.wait_ge(s_tb, 1)
                    dve.tensor_copy(TB[:, :], PS[0][:, 0:NBATCH * E]).then_inc(s_set, 1)
                    dve.wait_ge(s_set, KD + 1)
                logits1(b)
                for i in range(CS):
                    gated(b, i, first)
                    if first and i < 3:
                        split_w(2 + i)
                    if not first and i < 2:
                        combine(b - 1, STEPS - 2 + i, False)
                    if not first and i == 1:
                        times_rms(b - 1)
                    if i == 2:
                        route1(b)
                if first:
                    split_w(5)
                    split_w(6)
                for i in range(CS, STEPS):
                    low(b, i)
                    if i >= CS + 1:
                        combine(b, i - 2, first)
                    if i == CS + 1 and not first:
                        logits2(b - 1)
                if not first:
                    dve.wait_ge(s_ust, 16 * b)

            body(0, True)
            with dve.Fori(1, NB) as b:
                body(b, False)
            combine(NB - 1, STEPS - 2, False)
            combine(NB - 1, STEPS - 1, False)
            times_rms(NB - 1)
            logits2(NB - 1)

            n_link = [0]

            def link(ins):
                n_link[0] += 1
                ins.then_inc(s_v, 1)
                dve.wait_ge(s_v, n_link[0])

            def te(a):
                return a.rearrange("p (t e) -> p t e", e=E)

            def wide(a, n):
                return a.unsqueeze(2).broadcast_to([P, a.shape[1], n])

            def rows(a, n):
                return a.unsqueeze(1).broadcast_to([P, n, a.shape[1]])

            rv = [RV[:, n * T:(n + 1) * T] for n in range(8)]
            RS0, TMP, RS, MX, SUM, SCORE, POS, PLACE = rv
            dve.wait_ge(s_ms, BT * NB)
            dve.tensor_scalar(MSQ, MS[:, :], 1.0 / D, EPS2, ALU.mult, ALU.add).then_inc(s_msq, 1)
            dve.wait_ge(s_va, 1)
            link(dve.reciprocal(RS0, SQ))
            link(dve.tensor_tensor(TMP, RS0, RS0, ALU.mult))
            link(dve.tensor_tensor(TMP, TMP, MSQ, ALU.mult))
            link(dve.tensor_scalar(TMP, TMP, -0.5, 1.5, ALU.mult, ALU.add))
            link(dve.tensor_tensor(RS, RS0, TMP, ALU.mult))
            dve.wait_ge(s_lc, NB)
            link(dve.tensor_tensor(te(W8[0]), te(LOG[:, :]), wide(RS, E), ALU.mult))
            link(dve.tensor_reduce(MX, te(W8[0]), AX, ALU.max))
            dve.tensor_tensor(te(W8[1]), te(W8[0]), wide(MX, E), ALU.subtract).then_inc(s_diff, 1)
            dve.wait_ge(s_diff, 1)
            link(dve.tensor_scalar(W8[0], W8[1], 0.0, None, ALU.is_ge))
            link(dve.tensor_tensor(te(W8[3]), te(W8[0]), rows(REV[:, :], T), ALU.mult))
            link(dve.tensor_reduce(MX, te(W8[3]), AX, ALU.max))
            dve.tensor_tensor(te(OHB[:, :]), te(W8[3]), wide(MX, E), ALU.is_equal).then_inc(s_ohb, 1)
            link(dve.tensor_tensor(te(W8[0]), te(W8[3]), wide(MX, E), ALU.is_equal))
            dve.wait_ge(s_va, 2)
            link(dve.tensor_reduce(SUM, te(W8[2]), AX, ALU.add))
            link(dve.reciprocal(SCORE, SUM))
            CNT, NT, END, BEG, ONE8 = (CE[:, n * E:(n + 1) * E] for n in range(5))
            dve.wait_ge(s_rank, 1)
            link(dve.tensor_reduce(CNT, PF[1][:, 0:T * E].rearrange("p (t e) -> p e t", e=E), AX, ALU.add))
            link(dve.tensor_tensor(TE.rearrange("p (e t) -> p e t", t=T), wide(CNT, T), rows(THR[:, 0:T], E), ALU.is_gt))
            link(dve.tensor_reduce(NT, TE.rearrange("p (e t) -> p e t", t=T), AX, ALU.add))
            link(dve.tensor_scalar(NT, NT, 1.0, None, ALU.max))
            link(dve.tensor_tensor_scan(END, ONES[:, 0:E], NT, 0.0, ALU.mult, ALU.add))
            link(dve.tensor_tensor(BEG, END, NT, ALU.subtract))
            link(dve.tensor_scalar(BEG, BEG, float(P), None, ALU.mult))
            link(dve.tensor_tensor(te(W8[3]), te(PF[0][:, 0:T * E]), rows(BEG, T), ALU.add))
            link(dve.tensor_tensor(W8[3], W8[3], W8[0], ALU.mult))
            link(dve.tensor_reduce(POS, te(W8[3]), AX, ALU.add))
            ge = GE.rearrange("p (t j) -> p t j", j=JC + 1)
            link(dve.tensor_tensor(ge, wide(POS, JC + 1), rows(THR[:, :], T), ALU.is_ge))
            link(dve.tensor_reduce(PLACE, ge, AX, ALU.add))
            link(dve.scalar_tensor_tensor(PLACE, PLACE, -float(P), POS, ALU.mult, ALU.add))
            link(dve.tensor_scalar(PLACE, PLACE, float(P), None, ALU.add))
            vv = VV.rearrange("p (t q j) -> p t q j", q=4, j=ST)
            link(dve.tensor_tensor(vv[:, :, 1, :], ge[:, :, 0:ST], ge[:, :, 1:ST + 1], ALU.subtract))
            link(dve.tensor_tensor(vv[:, :, 0, :], vv[:, :, 1, :], wide(TOK[:, :], ST), ALU.mult))
            link(dve.tensor_tensor(vv[:, :, 2, :], vv[:, :, 1, :], wide(SCORE, ST), ALU.mult))
            link(dve.tensor_tensor(vv[:, :, 3, :], vv[:, :, 1, :], wide(RS, ST), ALU.mult))
            for h in range(4):
                dve.tensor_tensor(AOH[:, h * 512:(h + 1) * 512].rearrange("p (t c) -> p t c", c=P),
                                  rows(IOTA[:, :], 4), wide(PLACE[:, 4 * h:4 * h + 4], P),
                                  ALU.is_equal).then_inc(s_aoh, 1)
            ET, A1, A2, SL = (TF[:, n * JC:(n + 1) * JC] for n in range(4))
            link(dve.tensor_tensor(TJ.rearrange("p (j e) -> p j e", e=E), wide(IOTA[:, 0:JC], E), rows(END, JC), ALU.is_ge))
            link(dve.tensor_reduce(ET, TJ.rearrange("p (j e) -> p j e", e=E), AX, ALU.add))
            link(dve.tensor_scalar(ET, ET, float(E - 1), None, ALU.min))
            link(dve.tensor_scalar(A1, ET, float(NSLOT), -float(NSLOT), ALU.is_ge, ALU.mult))
            link(dve.tensor_scalar(A2, ET, 2.0 * NSLOT, -float(NSLOT), ALU.is_ge, ALU.mult))
            link(dve.tensor_tensor(SL, ET, A1, ALU.add))
            link(dve.tensor_tensor(SL, SL, A2, ALU.add))
            tab = TAB[:, :].rearrange("p (j n) -> p j n", n=NCOL)
            link(dve.tensor_scalar(tab[:, :, C_NEED], ET, 1.0, None, ALU.add))
            link(dve.tensor_scalar(tab[:, :, C_WOFF], SL, float(SLOT), None, ALU.mult))
            link(dve.tensor_scalar(tab[:, :, C_BOFF], SL, float(BW), None, ALU.mult))
            link(dve.tensor_scalar(tab[:, :, C_PEXP], ET, 2.0, None, ALU.add))
            link(dve.tensor_scalar(A1, SL, 1.0, -float(NSLOT), ALU.is_ge, ALU.mult))
            link(dve.tensor_tensor(A1, A1, SL, ALU.add))
            link(dve.tensor_scalar(tab[:, :, C_POFF], A1, 2.0, float(SLOT), ALU.add, ALU.mult))
            link(dve.tensor_tensor(A1[:, 1:JC], ET[:, 1:JC], ET[:, 0:JC - 1], ALU.not_equal))
            link(dve.tensor_scalar(A2, ET, E - 2.5, None, ALU.is_lt))
            link(dve.tensor_tensor(tab[:, 1:JC, C_PREP], A1[:, 1:JC], A2[:, 1:JC], ALU.mult))
            link(dve.tensor_scalar(tab[:, 0:1, C_PREP], A2[:, 0:1], 0.0, None, ALU.mult))
            dve.wait_ge(s_sort, 1)
            link(dve.tensor_copy(SRT[:, :], PF[2][:, 0:4 * ST]))
            link(dve.tensor_copy(GID[:, :], SRT[:, 0:ST]))
            link(dve.tensor_scalar(SIDF[:, :], SRT[:, ST:2 * ST], -2.0 * N, 2.0 * N, ALU.mult, ALU.add))
            dve.tensor_tensor(SID[:, :], SIDF[:, :], SRT[:, 0:ST], ALU.add).then_inc(s_route, 1)
            dve.wait_ge(s_route, 1)

            def col(a, i, c):
                return dve.value_load(TAB[0:1, bass.ds((4 * i + c) * NCOL + a, 1)], min_val=0, max_val=MOST[a])

            def low_x(i, c):
                dve.wait_ge(s_xh, 4 * i + c + 1)
                x0 = c % 2 * D
                dve.tensor_tensor(XL[:, x0:x0 + D], PF[2][:, 0:D], XH[:, x0:x0 + D].bitcast(F32),
                                  ALU.subtract).then_inc(s_xl, 1)

            def rows_out(i, c):
                j = 4 * i + c
                r = c % RX
                off = col(C_BOFF, i, c)
                dve.wait_ge(s_y, j + 1)
                if c >= 1:
                    dve.wait_ge(s_o, j)
                dve.tensor_tensor(YB, PS[c % 2][:, 0:D], BIAS[:, bass.ds(off + F, D)], ALU.add).then_inc(s_yb, 1)
                dve.wait_ge(s_yb, j + 1)
                if c >= RX:
                    dve.wait_ge(s_scatter[r], 16 * (i + c // RX))
                dve.scalar_tensor_tensor(OUTB[:, r * D:(r + 1) * D], YB, SRT[:, bass.ds(2 * ST + j, 1)],
                                         XG[:, (2 * r + 1) * D:(2 * r + 2) * D],
                                         ALU.mult, ALU.add).then_inc(s_o, 1)

            def step(i, c):
                j = 4 * i + c
                need, off = col(C_NEED, i, c), col(C_BOFF, i, c)
                dve.wait_ge(s_bias, 32 * need)
                for h in range(2):
                    dve.wait_ge(s_f2, 2 * j + h + 1)
                    if c >= 2:
                        dve.wait_ge(s_ht, 2 * j + h - 3)
                    a = c % 2 * F + h * 512
                    dve.scalar_tensor_tensor(AU[:, a:a + 512], PF[h][:, :], SRT[:, bass.ds(3 * ST + j, 1)],
                                             BIAS[:, bass.ds(off + h * 512, 512)],
                                             ALU.mult, ALU.add).then_inc(s_z, 1)
                if c + 1 < ST:
                    low_x(i, c + 1)
                if c >= 1:
                    rows_out(i, c - 1)
                for h in range(2):
                    dve.wait_ge(s_h2h, 2 * j + h + 1)
                    a = c % 2 * F + h * 512
                    dve.tensor_tensor(HL[:, a:a + 512], HF[:, a:a + 512], HH[:, a:a + 512].bitcast(F32),
                                      ALU.subtract).then_inc(s_h2, 1)

            low_x(0, 0)
            sorted_tiles(dve, step)
            rows_out(0, ST - 1)

        @block.tensor
        def _(pe):
            def three(out_ap, lhs, rhs, start, stop, shared=False):
                (ah, al), (bh, bl) = lhs, rhs
                pe.matmul(out_ap, ah, bh, start=start, stop=False, skip_group_check=shared)
                pe.matmul(out_ap, ah, bl, start=False, stop=False, skip_group_check=shared)
                return pe.matmul(out_ap, al, bh, start=False, stop=stop, skip_group_check=shared)

            def first_product(b, kind, i, first):
                wait_slot_read(pe, b, kind, i, first)
                for k in range(KD):
                    piece, col = w_first(kind, i, k)
                    if first:
                        pe.wait_ge(s_wsplit, 2 * piece + 2)
                    last = three(f_bank(kind, i)[:, :], (hi1(piece, col, P), lo1(piece, col, P)),
                                 (XH[:, k * BC:(k + 1) * BC], XL[:, k * BC:(k + 1) * BC]),
                                 k == 0, k == KD - 1)
                last.then_inc(s_f, 1)

            def second_product(b, i, first):
                pe.wait_ge(s_h, STEPS * b + i + 1)
                piece, col = w_second(i)
                if first:
                    pe.wait_ge(s_wsplit, 2 * piece + 2)
                w = (hi1(piece, col, D), lo1(piece, col, D))
                for t in range(BT):
                    if t % 2 == 0:
                        if i == 0 and not first:
                            pe.wait_ge(s_comb, comb_event(b - 1, STEPS - 1, t + 1))
                        elif i in (CS, CS + 1) and (i > CS or not first):
                            pe.wait_ge(s_comb, comb_event(b, CS - 1, t) if i > CS else comb_event(b - 1, STEPS - 2, t + 1))
                        elif i > CS + 1:
                            pe.wait_ge(s_comb, comb_event(b, i - 2, t + 1))
                    h = i % 4 * BC + t * P
                    dst = s_pair(i)[t // 2][:, t % 2 * D:(t % 2 + 1) * D]
                    shared = i < CS
                    last = three(dst, (HH[:, h:h + P], HL[:, h:h + P]), w,
                                 (i == 0 and t % 2 == 0) if shared else True,
                                 i == CS - 1 or not shared, shared)
                    if t == BT - 1 or t % 2 and i >= CS - 1:
                        last.then_inc(s_s, 1)

            def router1(b, first):
                pe.wait_ge(s_x, 16 * (b + 1))
                wait_slot_read(pe, b, "R", 0, first)
                for t in range(BT):
                    for k in range(KD):
                        last = pe.matmul(f_bank("R", 0)[:, t * E:(t + 1) * E],
                                         XR[:, k * BC + t * P:k * BC + (t + 1) * P], RW[:, k * E:(k + 1) * E],
                                         start=k == 0, stop=k == KD - 1)
                last.then_inc(s_r, 1)

            def transpose_u(b):
                pe.wait_ge(s_u, b + 1)
                for k in range(KD):
                    if isinstance(b, int):
                        pe.wait_ge(s_act, STEPS * NB)
                    else:
                        wait_slot_read(pe, b + 1, "T", k, False)
                    for t in range(BT):
                        last = pe.transpose(f_bank("T", k)[:, t * P:(t + 1) * P],
                                            U[:, t * D + k * P:t * D + (k + 1) * P], IDENT[:, :])
                    last.then_inc(s_t, 1)

            def router2(b):
                pe.wait_ge(s_ut, KD * (b + 1))
                if not isinstance(b, int):
                    wait_slot_read(pe, b + 1, "L", 0, False)
                for t in range(BT):
                    for k in range(KD):
                        last = pe.matmul(f_bank("L", 0)[:, t * E:(t + 1) * E],
                                         UT[:, k * BC + t * P:k * BC + (t + 1) * P], GW[:, k * E:(k + 1) * E],
                                         start=k == 0, stop=k == KD - 1)
                last.then_inc(s_l, 1)

            def body(b, first):
                router1(b, first)
                pe.wait_ge(s_xsplit, 2 * b + 2)
                for i in range(STEPS):
                    for kind in ("ab" if i < CS else "e"):
                        first_product(b, kind, i if i < CS else i - CS, first)
                    if i >= 2:
                        second_product(b, i - 2, first)
                    elif not first:
                        second_product(b - 1, STEPS - 2 + i, False)
                    if i == CS - 1 and not first:
                        transpose_u(b - 1)
                    if i == CS + 1 and not first:
                        router2(b - 1)

            pe.wait_ge(s_set, KD)
            pe.wait_ge(s_pool, 10)
            for k in range(KD):
                last = pe.matmul(PS[0][:, 0:NBATCH * E], ONES[:, :],
                                 PCB[:, k * NBATCH * E:(k + 1) * NBATCH * E], start=k == 0, stop=k == KD - 1)
            last.then_inc(s_tb, 1)
            body(0, True)
            with pe.Fori(1, NB) as b:
                body(b, False)
            second_product(NB - 1, STEPS - 2, False)
            second_product(NB - 1, STEPS - 1, False)
            transpose_u(NB - 1)
            router2(NB - 1)

            pe.wait_ge(s_ohb, 1)
            pe.matmul(PF[0][:, 0:T * E], TRI[:, :], OHB[:, :], start=True, stop=False, skip_group_check=True)
            for t in range(T - 1):
                n = T - 1 - t
                pe.matmul(PF[0][:, (t + 1) * E:T * E], ONEB[:, :],
                          OHB[:, t * E:(t + 1) * E].unsqueeze(1).broadcast_to([P, n, E]),
                          start=False, stop=t == T - 2, skip_group_check=True)
            pe.matmul(PF[1][:, 0:T * E], ONEB[:, :], OHB[:, :], start=True, stop=True).then_inc(s_rank, 1)
            for t in range(T):
                pe.wait_ge(s_aoh, t // 4 + 1)
                last = pe.matmul(PF[2][:, 0:4 * ST], AOH[:, t * P:(t + 1) * P], VV[:, t * 4 * ST:(t + 1) * 4 * ST],
                                 start=t == 0, stop=t == T - 1)
            last.then_inc(s_sort, 1)

            def col(a, i, c):
                return pe.value_load(TAB[0:1, bass.ds((4 * i + c) * NCOL + a, 1)], min_val=0, max_val=MOST[a])

            def transpose_x(i, c):
                r = c % RX
                pe.wait_ge(s_gather[r], 16 * (i + c // RX + 1))
                if c >= 1:
                    pe.wait_ge(s_xl, 4 * i + c)
                for k in range(KD):
                    last = pe.transpose(PF[2][:, k * P:(k + 1) * P],
                                        XG[:, 2 * r * D + k * P:2 * r * D + (k + 1) * P], IDENT[:, :])
                last.then_inc(s_xt, 1)

            def hidden(i, c):
                j = 4 * i + c
                need, off = col(C_NEED, i, c), col(C_WOFF, i, c)
                pe.wait_ge(s_lo, NPE * need)
                pe.wait_ge(s_xl, j + 1)
                for h in range(2):
                    if c >= 1:
                        pe.wait_ge(s_z, 2 * j + h - 1)
                    for k in range(KD):
                        x0 = c % 2 * D + k * P
                        w0 = off + k * F + h * 512
                        last = three(PF[h][:, :], (XH[:, x0:x0 + P], XL[:, x0:x0 + P]),
                                     (WA[:, bass.ds(w0, 512)], WA[:, bass.ds(w0 + NPE * PC, 512)]),
                                     k == 0, k == KD - 1)
                    last.then_inc(s_f2, 1)

            def project(i, c):
                j = 4 * i + c
                off = col(C_WOFF, i, c)
                if c >= 2:
                    pe.wait_ge(s_yb, j - 1)
                for n in range(CF):
                    if n % (CF // 2) == 0:
                        pe.wait_ge(s_h2, 2 * j + n // (CF // 2) + 1)
                    h0 = c % 2 * F + n * P
                    w0 = off + 2 * PC + n * D
                    last = three(PS[c % 2][:, 0:D], (HH[:, h0:h0 + P], HL[:, h0:h0 + P]),
                                 (WA[:, bass.ds(w0, D)], WA[:, bass.ds(w0 + NPE * PC, D)]), n == 0, n == CF - 1)
                last.then_inc(s_y, 1)

            def transpose_z(i, c):
                j = 4 * i + c
                for h in range(2):
                    pe.wait_ge(s_z, 2 * j + h + 1)
                    if c >= 1:
                        pe.wait_ge(s_si2, 2 * j + h - 1)
                    for n in range(4):
                        z0 = c % 2 * F + h * 512 + n * P
                        last = pe.transpose(PS[2 + h][:, n * P:(n + 1) * P], AU[:, z0:z0 + P], IDENT[:, :])
                    last.then_inc(s_ht, 1)

            def step(i, c):
                hidden(i, c)
                if c + 1 < ST:
                    transpose_x(i, c + 1)
                if c >= 1:
                    project(i, c - 1)
                transpose_z(i, c)

            pe.wait_ge(s_route, 1)
            transpose_x(0, 0)
            sorted_tiles(pe, step)
            project(0, ST - 1)


def kernel(**inputs):
    import concourse.bacc as bacc
    from concourse.bass_utils import run_bass_kernel_spmd as run

    a = {k: np.asarray(v) for k, v in inputs.items()}
    B, S, D = a["x"].shape
    P = 128

    def features_first(m):
        return np.ascontiguousarray(m.T.reshape(m.shape[1] // P, P, m.shape[0]).transpose(1, 0, 2))

    E, hr, _ = a["L0_cond_rw1"].shape
    arrays = {
        "x": np.ascontiguousarray(a["x"].reshape(B * S, D)),
        "xT": features_first(a["x"].reshape(B * S, D)),
        "condT": features_first(a["cond_1024"]),
        "routerT": features_first(a["L0_cond_router_w"]),
        "router_tT": features_first(a["L0_cond_router_t_w"]),
        "router_bias": np.ascontiguousarray(a["L0_cond_router_bias"]),
        "sw1T": features_first(a["L0_cond_sw1"]),
        "sw3T": features_first(a["L0_cond_sw3"]),
        "sw2T": features_first(a["L0_cond_sw2"]),
        "rw1T": features_first(a["L0_cond_rw1"].reshape(E * hr, D)),
        "rw2T": np.ascontiguousarray(a["L0_cond_rw2"].transpose(2, 0, 1)),
        "rms_row": np.ascontiguousarray(a["L0_ffn_rms_w"]),
        "gateT": features_first(a["L0_ffn_gate_w"]),
        "W1": np.ascontiguousarray(a["L0_ffn_W1"]),
        "b1": np.ascontiguousarray(a["L0_ffn_b1"]),
        "W2": np.ascontiguousarray(a["L0_ffn_W2"]),
        "b2": np.ascontiguousarray(a["L0_ffn_b2"]),
    }
    nc = bacc.Bacc("TRN2", target_bir_lowering=False, num_devices=1)
    args = [nc.dram_tensor(n, v.shape, mybir.dt.from_np(v.dtype), kind="ExternalInput").ap()
            for n, v in arrays.items()]
    out = nc.dram_tensor("out", (B * S, D), F32, kind="ExternalOutput").ap()
    scratch = nc.dram_tensor("scratch", (B * S, 2 * D), F32, kind="Internal").ap()
    build(nc, *args, out, scratch)
    got = run(nc, [arrays], core_ids=[0]).results[0]["out"]
    return got.reshape(B, S, D)
```
